# Optimizing a Trainium2 kernel written in Bass

```python
import numpy as np
import jax
import jax.numpy as jnp

def _softmax(x, axis=-1):
    return jax.nn.softmax(x, axis=axis)
def _gelu(x):
    return jax.nn.gelu(x, approximate=True)
def _silu(x):
    return jax.nn.silu(x)
def _sigmoid(x):
    return jax.nn.sigmoid(x)
def _layernorm(x, axis=-1, eps=1e-5):
    m = jnp.mean(x, axis=axis, keepdims=True)
    v = jnp.var(x, axis=axis, keepdims=True)
    return (x - m) / jnp.sqrt(v + eps)
def _scatter_add(tgt, idx, src, axis=0):
    return tgt.at[idx].add(src)
def _segment_sum(src, seg, n):
    return jax.ops.segment_sum(src, seg, n)

kernel_name = 'mk_conv_preact_d2_conv_nchw64_956b12'

def setup_inputs(seed: int = 0):
    np.random.seed(seed)
    _w = jnp.asarray
    def _rec_inputs():
        import jax
        import jax.numpy as jnp
        _gk = jax.random.key(seed)
        x = -7.109e-05 + 0.9999 * jax.random.normal(jax.random.fold_in(_gk, 1), (16, 64, 256, 256), jnp.float32)
        return x
    x = _rec_inputs()
    def _L0_conv_setup():
        import jax, jax.numpy as jnp
        import numpy as np
        N_HEADS = 4
        key = jax.random.key(seed)
        k1, k2, k3 = jax.random.split(key, 3)
        x = jax.random.normal(k1, (16, 64, 256, 256), dtype=jnp.float32)
        weight_re = jax.random.normal(k2, (4, 16, 16, 32, 17), dtype=jnp.float32) * 0.01
        weight_im = jax.random.normal(k3, (4, 16, 16, 32, 17), dtype=jnp.float32) * 0.01
        bias = jnp.zeros((64, 1, 1), dtype=jnp.float32)
        return {'x': x, 'weight_re': weight_re, 'weight_im': weight_im, 'bias': bias}
    _L0_conv_all = _L0_conv_setup()
    _L0_conv_in = {k: v for k, v in _L0_conv_all.items() if k in ('weight_re', 'weight_im', 'bias', )}
    del _L0_conv_all

    def _L1_conv_setup():
        import jax, jax.numpy as jnp
        import numpy as np
        B, C, H, W = (64, 64, 64, 64)
        EPS = 1e-05
        key = jax.random.key(seed)
        k1, k2 = jax.random.split(key)
        xs = 0.5 * jax.random.normal(k1, (B, C - 1, H, W), dtype=jnp.float32)
        x0 = jnp.sqrt(1.0 + jnp.sum(xs * xs, axis=1, keepdims=True))
        x = jnp.concatenate([x0, xs], axis=1)
        gamma = 0.5 + jax.random.uniform(k2, (C - 1,), dtype=jnp.float32)
        beta = 0.05 * jax.random.normal(jax.random.fold_in(key, 7), (C - 1,), dtype=jnp.float32)
        return {'x': x, 'gamma': gamma, 'beta': beta}
    _L1_conv_all = _L1_conv_setup()
    _L1_conv_in = {k: v for k, v in _L1_conv_all.items() if k in ('gamma', 'beta', )}
    del _L1_conv_all

    return {
        "x": x,
        "L0_conv_weight_re": _L0_conv_in["weight_re"],
        "L0_conv_weight_im": _L0_conv_in["weight_im"],
        "L0_conv_bias": _L0_conv_in["bias"],
        "L1_conv_gamma": _L1_conv_in["gamma"],
        "L1_conv_beta": _L1_conv_in["beta"],
    }

def reference(x, L0_conv_weight_re, L0_conv_weight_im, L0_conv_bias, L1_conv_gamma, L1_conv_beta):
    import jax
    import jax.numpy as jnp
    def _L0_conv_ref(x, weight_re, weight_im, bias):
        import jax, jax.numpy as jnp
        import numpy as np
        N_HEADS = 4
        B, C, H, W = x.shape
        weight = weight_re + 1j * weight_im
        n_heads = weight.shape[0]
        head_in = C // n_heads
        head_out = weight.shape[2]
        x_freq = jnp.fft.rfft2(x, axes=(-2, -1))
        fH, fW = (x_freq.shape[-2], x_freq.shape[-1])
        m_x = min(weight.shape[-2], fH)
        m_y = min(weight.shape[-1], fW)
        xf = x_freq.reshape(B, n_heads, head_in, fH, fW)
        core = jnp.einsum('bhixy,hioxy->bhoxy', xf[:, :, :, :m_x, :m_y], weight[:, :, :, :m_x, :m_y])
        out_freq = jnp.zeros((B, n_heads, head_out, fH, fW), dtype=core.dtype)
        out_freq = out_freq.at[:, :, :, :m_x, :m_y].set(core)
        out_freq = out_freq.reshape(B, n_heads * head_out, fH, fW)
        x_out = jnp.fft.irfft2(out_freq, s=(H, W), axes=(-2, -1))
        return x_out + bias

    def _L1_conv_ref(x, gamma, beta):
        import jax, jax.numpy as jnp
        import numpy as np
        B, C, H, W = (64, 64, 64, 64)
        EPS = 1e-05
        Bn, Cn, Hn, Wn = x.shape
        xf = x.transpose(0, 2, 3, 1).reshape(-1, Cn)
        m = jnp.mean(xf, axis=0)
        mm = m[0] * m[0] - jnp.sum(m[1:] * m[1:])
        mu = m / jnp.sqrt(jnp.maximum(mm, EPS))
        alpha = xf[:, 0] * mu[0] - xf[:, 1:] @ mu[1:]
        alpha = jnp.maximum(alpha, 1.0 + EPS)
        d = jnp.arccosh(alpha)
        var = jnp.mean(d * d)
        coef = d / jnp.sqrt(alpha * alpha - 1.0)
        v = coef[:, None] * (xf - alpha[:, None] * mu[None, :])
        mu_plus_o = mu.at[0].add(1.0)
        vo = v - (v[:, 0] / (1.0 + mu[0]))[:, None] * mu_plus_o[None, :]
        vs = vo[:, 1:]
        s = gamma[None, :] * vs / (jnp.sqrt(var) + EPS) + beta[None, :]
        t = jnp.sqrt(1.0 + jnp.sum(s * s, axis=1, keepdims=True))
        out = jnp.concatenate([t, s], axis=1)
        return out.reshape(Bn, Hn, Wn, Cn).transpose(0, 3, 1, 2)

    def _gn(v, G=32, eps=1e-5):
        B_, C_, H_, W_ = v.shape
        g = v.reshape(B_, G, C_ // G, H_, W_)
        m = jnp.mean(g, axis=(2, 3, 4), keepdims=True)
        s = jnp.var(g, axis=(2, 3, 4), keepdims=True)
        return ((g - m) / jnp.sqrt(s + eps)).reshape(v.shape)

    def _ln_c(v, eps=1e-6):
        m = jnp.mean(v, axis=1, keepdims=True)
        s = jnp.var(v, axis=1, keepdims=True)
        return (v - m) / jnp.sqrt(s + eps)

    def _ln_t(v, eps=1e-5):
        m = jnp.mean(v, axis=-1, keepdims=True)
        s = jnp.var(v, axis=-1, keepdims=True)
        return (v - m) / jnp.sqrt(s + eps)

    def _to_tokens(v):
        B_, C_, H_, W_ = v.shape
        return v.reshape(B_, C_, H_ * W_).transpose(0, 2, 1)
    def _from_tokens(t, like):
        B_, C_, H_, W_ = like.shape
        return t.transpose(0, 2, 1).reshape(B_, C_, H_, W_)

    x = x + _L0_conv_ref(_gn(x), L0_conv_weight_re, L0_conv_weight_im, L0_conv_bias)
    x = x + _L1_conv_ref(_gn(x), L1_conv_gamma, L1_conv_beta)
    return x


_drawn_inputs = setup_inputs


def setup_inputs(seed=0):
    import zlib

    import numpy as np

    out = dict(_drawn_inputs(seed))
    spreads = {'L0_conv_bias': (0.0, 0.1)}
    factors = {'L0_conv_weight_re': 6.432, 'L0_conv_weight_im': 6.292, 'L1_conv_beta': 2.694}
    for name, (base, spread) in spreads.items():
        noise = np.random.default_rng([zlib.crc32(name.encode()), seed]).standard_normal(out[name].shape)
        drawn = base * np.exp(spread * noise) if base else spread * noise
        out[name] = jnp.asarray(drawn.astype(out[name].dtype))
    for name, factor in factors.items():
        out[name] = (out[name] * factor).astype(out[name].dtype)
    return out
```

```python
import concourse.bass as bass
from concourse import mybir
from contextlib import ExitStack

FP32 = mybir.dt.float32
BF16 = mybir.dt.bfloat16
ALU = mybir.AluOpType
ACT = mybir.ActivationFunctionType
AX_X = mybir.AxisListType.X

C, H, W = 64, 256, 256
N = H * W
HALF = N // 2
HEADS, CI = 4, 16
KX, KY = 32, 17
M2 = 2 * KY
G = C // 2
GN_EPS = 1e-5
EPS = 1e-5
CONSTS = ("dft_h", "dft_w", "sel", "mode_w", "idft_h", "idft_w", "misc")


def constants():
    import numpy as np
    kx, ky = np.arange(KX), np.arange(KY)
    c = {}
    rows = np.arange(H).reshape(128, 2)
    th = 2 * np.pi * rows[:, :, None] * kx / H
    c["dft_h"] = np.concatenate([np.cos(th), -np.sin(th)], 2)
    cols = np.arange(W).reshape(2, 128).T
    tw = 2 * np.pi * cols[:, :, None] * ky / W
    t = np.zeros((128, 2, 2, 128))
    t[:, 0, :, :KY], t[:, 0, :, KY:M2] = np.cos(tw), -np.sin(tw)
    t[:, 1, :, :KY], t[:, 1, :, KY:M2] = np.sin(tw), np.cos(tw)
    c["dft_w"] = t
    p = np.arange(128)
    same = (p[:, None] // KX == p[None] // KX).astype(float)
    dc = same * (p[:, None] % KX == 0)
    c["sel"] = np.stack([np.ones((128, 128)), dc, same, np.repeat(p[:, None] % KX == 0, 128, 1),
                         np.repeat(p[:, None] == 0, 128, 1)], 1)
    e = np.full((128, 2, KY), 2.0)
    e[:, :, 0] = 0.5
    x = np.full((128, 2, KY), 2.0)
    x[:, :, 0] = 1.0
    e[p % KX == 0, :, 0] = 0.0
    x[p % KX == 0, :, 0] = 0.0
    c["mode_w"] = np.stack([e, 2 * x], 1)
    hh = 2 * np.pi * kx[:, None] * np.arange(H) / H
    ih = np.zeros((128, H))
    ih[:KX], ih[KX:2 * KX] = np.cos(hh), np.sin(hh)
    c["idft_h"] = ih
    w = 2 * np.pi * ky[:, None] * np.arange(W) / W
    scale = np.where(ky == 0, 1.0, 2.0)[:, None] / N
    iw = np.zeros((128, W))
    iw[:KY], iw[KY:M2] = scale * np.cos(w), -scale * np.sin(w)
    iw[KY] = 0.0
    c["idft_w"] = iw
    m = np.zeros((128, 48))
    m[:, 0:4] = p[:, None] // KX == np.arange(4)
    m[:, 4] = np.where(p % KX == 0, -float(N), 0.0)
    for s in range(2):
        m[:, 8 + s] = p % 2 == s
    m[:, 10] = np.where(p // 2 == 0, 1.0, -1.0)
    for block, (first, maps) in enumerate(((0, 6), (12, 4), (20, 2))):
        for k in range(maps):
            for s in range(2):
                m[first + 2 * k + s, 12 + 6 * (k % 2) + 2 * block + s] = 1.0
    for part in range(3):
        m[32 + part, 24 + 2 * part:26 + 2 * part] = 1.0
    for s in range(2):
        m[96 + s, 30 + s] = -1.0
    m[98, 32:34] = 1.0
    c["misc"] = m
    return {k: np.ascontiguousarray(v, dtype=np.float32) for k, v in c.items()}


def is_at(b, n):
    return isinstance(b, int) and b == n


class Sync:

    def __init__(self, sp, met):
        self.sp, self.met, self.dma_start, self.Fori = sp, met, sp.dma_start, sp.Fori

    def wait_ge(self, sem, value):
        if not isinstance(value, int):
            value = self.sp.to_reg(value)
            self.sp.wait_ge(self.met, 16)
        self.sp.wait_ge(sem, value)


class Chain:

    def __init__(self, eng, sem):
        self.eng, self.sem, self.done, self.reg = eng, sem, 0, None

    def inc(self, ins):
        ins.then_inc(self.sem, 1)
        self.done += 1

    def value(self):
        if self.reg is None:
            return self.done
        return self.reg * self.per + (self.done - self.first * self.per)

    def wait(self):
        self.eng.wait_ge(self.sem, self.value())

    def step(self, ins):
        self.inc(ins)
        self.wait()

    def loop(self, reg, first, per):
        self.reg, self.first, self.per, self.start = reg, first, per, self.done

    def end(self, turns):
        assert self.done - self.start == self.per, (self.done - self.start, self.per)
        self.done, self.reg = self.start + turns * self.per, None


def stage_a(nc, ctx, io, B):
    x, spec, stats, wmix, bias, cst = io["x"], io["spec"], io["stats"], io["wmix"], io["bias"], io["cst"]
    sem = lambda n: ctx.enter_context(nc.semaphore("a_" + n))
    NX = 4
    Q = C // 8
    x_v = x.rearrange("b (h q i) (p j) w -> b q i p h (j w)", h=HEADS, i=2, p=128)
    x_in = [sem(f"x_in{k}") for k in range(NX)]
    const_in, w_in, neg_w = sem("const_in"), sem("w_in"), sem("neg_w")
    rows_mm, rows_sb = sem("rows_mm"), sem("rows_sb")
    tr_mm, tr_sb = sem("tr_mm"), sem("tr_sb")
    cols_mm, cols_sb = sem("cols_mm"), sem("cols_sb")
    sq_done, sq_kept = sem("sq_done"), sem("sq_kept")
    sums_mm, energy, stat_mm = sem("sums_mm"), sem("energy"), sem("stat_mm")
    y_ready, y_out, st_ready, st_out, chain = sem("y_ready"), sem("y_out"), sem("st_ready"), sem("st_out"), sem("chain")
    sums_read, stat_read = sem("sums_read"), sem("stat_read")
    var1_ready, rstd1_ready, var2_ready, yrot_out = sem("var1_ready"), sem("rstd1_ready"), sem("var2_ready"), sem("yrot_out")
    chain_end, macc_out, powers = sem("chain_end"), sem("macc_out"), sem("powers")

    with ExitStack() as mem:
        sb = lambda n, s, d=FP32: mem.enter_context(nc.sbuf_tensor("a_" + n, s, d))
        ps = lambda n, s: mem.enter_context(nc.psum_tensor("a_" + n, s, FP32))
        xt = [sb(f"xt{k}", [128, HEADS, 2, 2 * W]) for k in range(NX)]
        dft_h = sb("dft_h", [128, 2, 64])
        dft_w = sb("dft_w", [128, 2, 2, 128])
        sel = sb("sel", [128, 5, 128])
        mode_w = sb("mode_w", [128, 2, M2])
        misc = sb("misc", [128, 48])
        ident = sb("ident", [128, 128])
        bias_t = sb("bias_t", [128, CI])
        wm = sb("wm", [128, CI, 2, CI * M2])
        rows = [[sb(f"rows{a}{i}", [128, 512]) for i in range(2)] for a in range(2)]
        cols = [[sb(f"cols{a}{i}", [128, 512]) for i in range(2)] for a in range(2)]
        junk = [sb(f"junk{k}", [128, 1024], BF16) for k in range(2)]
        sq = sb("sq", [128, Q, HEADS])
        sqk = sb("sqk", [128, Q, HEADS])
        xm = sb("xm", [128, CI, M2])
        xk = sb("xk", [128, CI, M2])
        xh = sb("xh", [128, CI, M2])
        prod = [sb(f"prod{k}", [128, 2, CI * M2]) for k in range(2)]
        y = sb("y", [128, CI, M2])
        yrot = sb("yrot", [128, CI, M2])
        t1, t2 = sb("t1", [128, CI, M2]), sb("t2", [128, CI, M2])
        sm = sb("sm", [128, 32, 16])
        st = sb("st", [128, 4, CI])
        p_rows = [ps(f"p_rows{i}", [128, 512]) for i in range(2)]
        p_tr = [ps(f"p_tr{i}", [128, 512]) for i in range(2)]
        p_cols = [ps(f"p_cols{a}", [128, 2, 128]) for a in range(2)]
        p_sums = ps("p_sums", [128, 512])
        p_stat = ps("p_stat", [128, 512])
        consts = ((dft_h, "dft_h"), (dft_w, "dft_w"), (sel, "sel"), (mode_w, "mode_w"), (misc, "misc"), (ident, "ident"))

        block = mem.enter_context(nc.Block())

        @block.sync
        def _(sp):
            sp = Sync(sp, const_in)
            for i, (t, name) in enumerate(consts[:2]):
                sp.dma_start(t[:], cst[name]).then_inc(const_in, 16)

            def store_modes(b):
                sp.wait_ge(y_ready, b * 2 + 2)
                sp.dma_start(spec[b, 0], y[:].rearrange("p i m -> p (i m)")).then_inc(y_out, 16)
                sp.dma_start(spec[b, 1], yrot[:].rearrange("p i m -> p (i m)")).then_inc(yrot_out, 16)

            def load(b, q):
                if not (isinstance(b, int) and 8 * b + q < NX):
                    sp.wait_ge(rows_mm, b * 16 + 2 * (q - NX) + 2)
                    sp.wait_ge(sq_done, b * 32 + 4 * (q - NX + 1))
                for i in range(2):
                    sp.dma_start(xt[q % NX][:, :, i], x_v[b, q, i]).then_inc(x_in[q % NX], 16)

            for q in range(2):
                load(0, q)
            for i, (t, name) in enumerate(consts[2:]):
                sp.dma_start(t[:], cst[name]).then_inc(const_in, 16)
            for h in range(HEADS):
                sp.dma_start(bias_t[KX * h:KX * h + KX], bias[CI * h:CI * h + CI].unsqueeze(0).to_broadcast((KX, CI))).then_inc(const_in, 16)
            for q in range(2, Q):
                load(0, q)
                if q == 3:
                    sp.dma_start(wm[:].rearrange("p o a n -> p (o a n)"), wmix).then_inc(w_in, 16)
            for q in range(Q):
                load(1, q)
            with sp.Fori(2, B) as b:
                for q in range(Q):
                    if q == 4:
                        store_modes(b - 2)
                    load(b, q)
            store_modes(B - 2)
            store_modes(B - 1)
            sp.wait_ge(y_out, B * 16)
            sp.wait_ge(yrot_out, B * 16)

        @block.tensor
        def _(pe):
            def row_dft(b, q):
                pe.wait_ge(x_in[q % NX], b * 64 + (q // NX) * 32 + 32)
                for i in range(2):
                    if not (is_at(b, 0) and q == 0):
                        pe.wait_ge(rows_sb, b * 16 + 2 * q + i - 1)
                    for j in range(2):
                        for t in range(2):
                            last = nc.tensor.matmul(p_rows[i][64 * t:64 * t + 64, :], dft_h[:, j], xt[q % NX][:, t::2, i, j * W:(j + 1) * W],
                                                    start=(j == 0), stop=(j == 1))
                    last.then_inc(rows_mm, 1)

            def transposes(b, q):
                for i in range(2):
                    pe.wait_ge(rows_sb, b * 16 + 2 * q + i + 1)
                    if not (is_at(b, 0) and q == 0):
                        pe.wait_ge(tr_sb, b * 16 + 2 * q + i - 1)
                    for hl in range(2):
                        for wh in range(2):
                            out = p_tr[i][:].rearrange("p (w r h k) -> p w h r k", w=2, r=2, h=4)[:, wh, 2 * hl:2 * hl + 2]
                            last = nc.tensor.transpose(out, rows[q % 2][i][:, 256 * hl + 128 * wh:256 * hl + 128 * wh + 128], ident[:])
                    last.then_inc(tr_mm, 1)

            def col_dft(b, q):
                if not (is_at(b, 0) and q < 2):
                    pe.wait_ge(cols_sb, b * 8 + q - 1)
                for i in range(2):
                    pe.wait_ge(tr_sb, b * 16 + 2 * q + i + 1)
                    v = cols[q % 2][i][:].rearrange("p (w r n) -> p w r n", w=2, r=2)
                    n = 0
                    for wh in range(2):
                        for r in range(2):
                            last = nc.tensor.matmul(p_cols[q % 2][:, i], v[:, wh, r], dft_w[:, r, wh], start=(n == 0), stop=(n == 3))
                            n += 1
                last.then_inc(cols_mm, 1)

            def first_sums(b):
                pe.wait_ge(sq_kept, b + 1)
                pe.wait_ge(cols_sb, b * 8 + 8)
                if not is_at(b, 0):
                    pe.wait_ge(sums_read, b)
                nc.tensor.matmul(p_sums[:, 0:32], sel[:, 0], sqk[:].rearrange("p q h -> p (q h)"), start=True, stop=True)
                nc.tensor.matmul(p_sums[:, 32:48], sel[:, 1], xm[:, :, 0], start=True, stop=True).then_inc(sums_mm, 1)

            def second_sums(b):
                pe.wait_ge(energy, b + 1)
                if not is_at(b, 0):
                    pe.wait_ge(stat_read, b)
                nc.tensor.matmul(p_stat[:, 0:16], sel[:, 2], sm[:, 8], start=True, stop=True)
                nc.tensor.matmul(p_stat[:, 16:32], sel[:, 1], y[:, :, 0], start=True, stop=True).then_inc(stat_mm, 1)

            def before(b, q, n):
                return (b, q - n) if q >= n else (b - 1, q - n + Q)

            def slot(b, q):
                row_dft(b, q)
                transposes(*before(b, q, 1))
                if q == 2 and not is_at(b, 0):
                    first_sums(b - 1)
                col_dft(*before(b, q, 2))
                if q == 2 and not (is_at(b, 0) or is_at(b, 1)):
                    second_sums(b - 2)

            pe.wait_ge(const_in, 32 + 16 * 8)
            row_dft(0, 0)
            row_dft(0, 1)
            transposes(0, 0)
            for q in range(2, Q):
                slot(0, q)
            for q in range(Q):
                slot(1, q)
            with pe.Fori(2, B) as b:
                for q in range(Q):
                    slot(b, q)
            transposes(B - 1, Q - 1)
            col_dft(B - 1, Q - 2)
            col_dft(B - 1, Q - 1)
            first_sums(B - 1)
            second_sums(B - 2)
            second_sums(B - 1)

        @block.scalar
        def _(act):
            def squares(b, q, h):
                if not (is_at(b, 0) and q == 0 and h < 2):
                    act.wait_ge(sq_done, b * 32 + 4 * q + h - 1)
                nc.scalar.activation(junk[h % 2][:].rearrange("p (i w) -> p i w", i=2), xt[q % NX][:, h], ACT.Square,
                                     accum_out=sq[:, q, h:h + 1]).then_inc(sq_done, 1)

            def copy_rows(b, q, i):
                act.wait_ge(rows_mm, b * 16 + 2 * q + i + 1)
                if not (is_at(b, 0) and q < 2):
                    act.wait_ge(tr_mm, b * 16 + 2 * q + i - 3)
                nc.scalar.activation(rows[q % 2][i][:], p_rows[i][:], ACT.Copy).then_inc(rows_sb, 1)

            def tile(b, q):
                act.wait_ge(x_in[q % NX], b * 64 + (q // NX) * 32 + 32)
                squares(b, q, 0)
                squares(b, q, 1)
                copy_rows(b, q, 0)
                squares(b, q, 2)
                squares(b, q, 3)
                copy_rows(b, q, 1)

            def keep(b):
                act.wait_ge(sq_done, b * 32 + 32)
                if not is_at(b, 0):
                    act.wait_ge(sums_mm, b)
                nc.scalar.activation(sqk[:], sq[:], ACT.Copy).then_inc(sq_kept, 1)
                act.wait_ge(sq_kept, b + 1)

            for q in range(Q):
                tile(0, q)
            keep(0)
            with act.Fori(1, B) as b:
                for q in range(Q):
                    tile(b, q)
                keep(b)

        @block.vector
        def _(dve):
            ch = Chain(dve, chain)
            row = lambda k, n=16: sm[:, k, 0:n]
            pair = lambda a: a.rearrange("p (g i) -> p g i", i=2)
            V = nc.vector

            def copy_tr(b, q):
                for i in range(2):
                    dve.wait_ge(tr_mm, b * 16 + 2 * q + i + 1)
                    if not (is_at(b, 0) and q < 2):
                        dve.wait_ge(cols_mm, b * 8 + q - 1)
                    V.tensor_copy(cols[q % 2][i][:], p_tr[i][:]).then_inc(tr_sb, 1)

            def copy_cols(b, q):
                dve.wait_ge(cols_mm, b * 8 + q + 1)
                if q == 0 and not is_at(b, 0):
                    dve.wait_ge(sums_mm, b)
                V.tensor_copy(xm[:, 2 * q:2 * q + 2], p_cols[q % 2][:, :, 0:M2]).then_inc(cols_sb, 1)

            def mix(q, waited=None):
                for o in (2 * q, 2 * q + 1):
                    ch.inc(V.tensor_tensor(prod[o % 2][:], wm[:, o], xh[:].rearrange("p i m -> p (i m)").unsqueeze(1).to_broadcast((128, 2, CI * M2)), ALU.mult))
                ch.wait()
                for o in (2 * q, 2 * q + 1):
                    if waited is not None and o == 0:
                        dve.wait_ge(y_out, waited)
                    ch.inc(V.tensor_reduce(y[:, o].rearrange("p (a k) -> p a k", a=2), prod[o % 2][:].rearrange("p a (n k) -> p a k n", k=KY), AX_X, ALU.add))
                ch.wait()

            def finish(b):
                bc = lambda k: mode_w[:, k].unsqueeze(1).to_broadcast((128, CI, M2))
                if not is_at(b, 0):
                    dve.wait_ge(yrot_out, b * 16)
                V.tensor_scalar(yrot[:, :, 0:KY], y[:, :, KY:M2], -1.0, None, ALU.mult).then_inc(y_ready, 1)
                V.tensor_copy(yrot[:, :, KY:M2], y[:, :, 0:KY]).then_inc(y_ready, 1)
                ch.inc(V.tensor_tensor(t1[:], y[:], bc(0), ALU.mult))
                ch.step(V.tensor_tensor(t2[:], xk[:], bc(1), ALU.mult))
                ch.step(V.tensor_tensor(t1[:], t1[:], t2[:], ALU.add))
                ch.step(V.tensor_tensor(t1[:], t1[:], y[:], ALU.mult))
                V.tensor_reduce(row(8), t1[:], AX_X, ALU.add).then_inc(energy, 1)

            def second_norm(b):
                dve.wait_ge(stat_mm, b + 1)
                ch.inc(V.tensor_reduce(row(9, 8), pair(p_stat[:, 0:16]), AX_X, ALU.add))
                ch.inc(V.tensor_tensor(row(11), row(3), row(3), ALU.mult))
                ins = V.tensor_tensor(row(10), p_stat[:, 16:32], row(3), ALU.add)
                ins.then_inc(stat_read, 1)
                dve.wait_ge(stat_read, b + 1)
                ch.step(V.scalar_tensor_tensor(out=row(10), in0=row(10), scalar=1.0 / N, in1=bias_t[:], op0=ALU.mult, op1=ALU.add))
                m = pair(row(10))
                ch.inc(V.tensor_tensor(row(12, 8), m[:, :, 0], m[:, :, 1], ALU.add))
                ch.inc(V.tensor_tensor(row(13, 8), m[:, :, 0], m[:, :, 1], ALU.subtract))
                ch.step(V.tensor_reduce(row(14, 8), pair(row(11)), AX_X, ALU.add))
                ch.step(V.scalar_tensor_tensor(out=row(15, 8), in0=row(14, 8), scalar=-1.0 / N, in1=row(2, 8), op0=ALU.mult, op1=ALU.add))
                ch.step(V.scalar_tensor_tensor(out=row(15, 8), in0=row(9, 8), scalar=1.0 / N, in1=row(15, 8), op0=ALU.mult, op1=ALU.add))
                ch.step(V.scalar_tensor_tensor(out=row(16, 8), in0=row(13, 8), scalar=0.25, in1=row(13, 8), op0=ALU.mult, op1=ALU.mult))
                ch.step(V.scalar_tensor_tensor(out=row(15, 8), in0=row(15, 8), scalar=0.5 / N, in1=row(16, 8), op0=ALU.mult, op1=ALU.add))
                ch.step(V.tensor_scalar(row(15, 8), row(15, 8), 0.0, GN_EPS, ALU.max, ALU.add))
                if not is_at(b, 0):
                    dve.wait_ge(st_out, b * 16)
                two = lambda a: a.unsqueeze(2).to_broadcast((128, 8, 2))
                V.tensor_copy(pair(st[:, 3]), two(row(15, 8))).then_inc(var2_ready, 1)
                V.tensor_scalar(pair(st[:, 1]), two(row(12, 8)), 0.5, None, ALU.mult).then_inc(var2_ready, 1)

            def mean_sum(b):
                dve.wait_ge(st_ready, b * 2 + 2)
                ch.step(V.scalar_tensor_tensor(out=row(17, 8), in0=row(13, 8), scalar=0.5, in1=pair(st[:, 0])[:, :, 0], op0=ALU.mult, op1=ALU.mult))
                a = pair(row(20))
                ch.inc(V.tensor_tensor(a[:, :, 0], a[:, :, 0], row(17, 8), ALU.add))
                ch.step(V.tensor_tensor(a[:, :, 1], a[:, :, 1], row(17, 8), ALU.subtract))

            def first_norm(b):
                dve.wait_ge(sums_mm, b + 1)
                parts = t2[:].rearrange("p i m -> p (i m)")[:, 0:32].rearrange("p (q h) -> p q h", h=4)
                ch.inc(V.tensor_tensor(parts, p_sums[:, 0:32].rearrange("p (q h) -> p q h", h=4),
                                       misc[:, 0:4].unsqueeze(1).to_broadcast((128, 8, 4)), ALU.mult))
                V.tensor_copy(row(27), p_sums[:, 32:48]).then_inc(sums_read, 1)
                dve.wait_ge(sums_read, b + 1)
                ch.inc(V.tensor_tensor(row(4, 8), pair(row(27))[:, :, 0], pair(row(27))[:, :, 1], ALU.add))
                ch.step(V.tensor_reduce(row(26, 8), parts, AX_X, ALU.add))
                ch.step(V.tensor_scalar(row(4, 8), row(4, 8), 0.5 / N, None, ALU.mult))
                ch.step(V.tensor_tensor(row(5, 8), row(4, 8), row(4, 8), ALU.mult))
                ch.step(V.scalar_tensor_tensor(out=row(6, 8), in0=row(26, 8), scalar=0.5 / N, in1=row(5, 8), op0=ALU.mult, op1=ALU.subtract))
                V.tensor_scalar(row(21, 8), row(6, 8), 0.0, GN_EPS, ALU.max, ALU.add).then_inc(var1_ready, 1)

            def start(b):
                ch.inc(V.tensor_copy(row(2, 8), row(26, 8)))
                ch.inc(V.tensor_copy(row(3), row(27)))
                ch.step(V.tensor_copy(xk[:], xm[:]))
                dve.wait_ge(rstd1_ready, b + 1)
                ch.inc(V.tensor_tensor(xh[:].rearrange("p (g i) m -> p g (i m)", i=2), xk[:].rearrange("p (g i) m -> p g (i m)", i=2),
                                       row(22, 8).unsqueeze(2).to_broadcast((128, 8, 2 * M2)), ALU.mult))
                ch.step(V.tensor_tensor(row(7, 8), row(4, 8), row(22, 8), ALU.mult))
                ch.step(V.tensor_scalar(row(7, 8), row(7, 8), misc[:, 4:5], None, ALU.mult))
                dcs = pair(xh[:, :, 0])
                ch.step(V.tensor_tensor(dcs, dcs, row(7, 8).unsqueeze(2).to_broadcast((128, 8, 2)), ALU.add))
                if not is_at(b, 0):
                    mean_sum(b - 1)

            ch.inc(V.memset(row(20), 0.0))
            dve.wait_ge(const_in, 32 + 16 * 8)
            copy_tr(0, 0)
            for q in range(Q):
                copy_tr(*((0, q + 1) if q + 1 < Q else (1, 0)))
                copy_cols(0, q)
                if q == 5:
                    dve.wait_ge(w_in, 16)
                    neg = wm[:, :, 0].rearrange("p o (i r k) -> p o i r k", r=2, k=KY)[:, :, :, 1]
                    ch.inc(V.tensor_scalar(neg, neg, -1.0, None, ALU.mult))
            first_norm(0)
            start(0)

            def entry(b, last=False):
                for q in range(Q):
                    if q and not (last and q + 1 == Q):
                        copy_tr(*((b, q + 1) if q + 1 < Q else (b + 1, 0)))
                    copy_cols(b, q)
                    mix(q, None if is_at(b, 1) or q else (b - 1) * 16)
                finish(b - 1)
                if not last:
                    copy_tr(b + 1, 1)
                first_norm(b)
                second_norm(b - 1)
                start(b)

            copy_tr(1, 1)
            entry(1)
            with dve.Fori(2, B - 1) as b:
                ch.loop(b, 2, PER_A)
                entry(b)
                ch.end(B - 3)
            entry(B - 1, last=True)
            for q in range(Q):
                mix(q, None if q else (B - 1) * 16)
            finish(B - 1)
            second_norm(B - 1)
            mean_sum(B - 1)
            V.memset(row(23), 0.0).then_inc(chain_end, 1)

        @block.gpsimd
        def _(pool):
            P = nc.gpsimd

            def first_rstd(b):
                pool.wait_ge(var1_ready, b + 1)
                P.tensor_tensor(sm[:, 22, 0:8], sm[:, 21, 0:8], sm[:, 24, 0:8], ALU.pow).then_inc(rstd1_ready, 1)

            def second_rstd(b):
                pool.wait_ge(var2_ready, b * 2 + 2)
                P.tensor_tensor(st[:, 0], st[:, 3], sm[:, 24], ALU.pow).then_inc(st_ready, 1)
                P.tensor_tensor(st[:, 2], st[:, 3], sm[:, 25], ALU.pow).then_inc(st_ready, 1)

            def store_stats(b):
                pool.wait_ge(st_ready, b * 2 + 2)
                pool.dma_start(stats[b].rearrange("s h i -> h s i"), st[0::KX, 0:3]).then_inc(st_out, 16)

            P.memset(sm[:, 24], -0.5).then_inc(powers, 1)
            P.memset(sm[:, 25], 0.5).then_inc(powers, 1)
            pool.wait_ge(powers, 2)
            first_rstd(0)
            with pool.Fori(1, B) as b:
                first_rstd(b)
                second_rstd(b - 1)
                store_stats(b - 1)
            second_rstd(B - 1)
            store_stats(B - 1)
            pool.wait_ge(chain_end, 1)
            pool.dma_start(io["macc"], sm[0::KX, 20]).then_inc(macc_out, 16)
            pool.wait_ge(st_out, B * 16)
            pool.wait_ge(macc_out, 16)


PER_A = 63

TB = 4096
TC = 2048


def stage_b(nc, ctx, io, B, keep):
    x, spec, stats, bias, cst = io["x"], io["spec"], io["stats"], io["bias"], io["cst"]
    sem = lambda n: ctx.enter_context(nc.semaphore("b_" + n))
    NX, T = 4, HALF // TB
    SL = T * TB // (4 * 512)
    x_v = x.rearrange("b c h w -> b (c h w)").rearrange("b (p t n) -> b t p n", p=128, t=T)
    x0_v = x.rearrange("b c (s h) w -> b c h s w", s=2)
    al_v = io["alx"].rearrange("b s (h w) -> b h s w", w=W)
    al_rows = io["alx"].rearrange("b s (k j n) -> b s j k n", j=4, n=512)
    x_in = [sem(f"x_in{k}") for k in range(NX)]
    c_in, setup, w_ready = sem("c_in"), sem("setup"), sem("w_ready")
    mm_done, pow_done, mean_ready = sem("mm_done"), sem("pow_done"), sem("mean_ready")
    al_mm, al_sb = sem("al_mm"), sem("al_sb")
    al_out = [sem(f"al_out{k}") for k in range(2)]
    al_in, x0_in, sp_in, sp_used = sem("al_in"), sem("x0_in"), sem("sp_in"), sem("sp_used")
    v_ready, z_mm, z_sb, y_mm = sem("v_ready"), sem("z_mm"), sem("z_sb"), sem("y_mm")
    alpha, chain, act_chain = sem("alpha"), sem("chain"), sem("act_chain")
    squares_ready, roots, logs, dsum_ready = sem("squares_ready"), sem("roots"), sem("logs"), sem("dsum_ready")
    e_ready, maps_ready, maps_out, beta_out, x10_out = sem("e_ready"), sem("maps_ready"), sem("maps_out"), sem("beta_out"), sem("x10_out")
    var_in, var_mm, std_ready, zeroed = sem("var_in"), sem("var_mm"), sem("std_ready"), sem("zeroed")
    uw_ready, uw_out, aw_ready, var_ready = sem("uw_ready"), sem("uw_out"), sem("aw_ready"), sem("var_ready")

    with ExitStack() as mem:
        sb = lambda n, s, d=FP32: mem.enter_context(nc.sbuf_tensor("b_" + n, s, d))
        ps = lambda n, s: mem.enter_context(nc.psum_tensor("b_" + n, s, FP32))
        xt = [sb(f"xt{k}", [128, TB]) for k in range(NX)]
        al_r = sb("al_r", [128, SL, 512])
        misc = sb("misc", [128, 48])
        ones = sb("ones", [128, 128])
        idft_h = sb("idft_h", [128, H])
        idft_w = sb("idft_w", [128, W])
        srow = sb("srow", [128, B, 3, C])
        mrow, brow, grow, btrow = sb("mrow", [128, C]), sb("brow", [128, C]), sb("grow", [128, C]), sb("btrow", [128, C])
        msr = sb("msr", [128, C])
        mcol, rcol = sb("mcol", [128, 1]), sb("rcol", [128, B])
        minus1 = sb("minus1", [128, 1])
        sc = sb("sc", [128, 16])
        arow = sb("arow", [128, B, C])
        aw, awc = sb("aw", [128, B, 32]), sb("awc", [128, 32])
        ac, q2, q3, dsum = sb("ac", [128, B]), sb("q2", [128, B]), sb("q3", [128, B]), sb("dsum", [128, B])
        v1, v2 = sb("v1", [128, B, C]), sb("v2", [128, B, C])
        vp = [sb(f"vp{k}", [128, B, C], BF16) for k in range(3)]
        wt = sb("wt", [128, B, C, 2], BF16)
        uw = sb("uw", [128, B, C, 2])
        spt = sb("spt", [64, C, M2])
        prod = sb("prod", [64, C, M2])
        vm = sb("vm", [128, 2, M2])
        zs = sb("zs", [M2, 2, H])
        dn = sb("dn", [128, 11, 512])
        ald, x0d, x10, al, t1, t2, w1, w2, dist, coef, beta = (dn[:, k] for k in range(11))
        wide = dn[:, 4:8].rearrange("p k n -> p (k n)")[:, 0:2 * B * C].rearrange("p (b c s) -> p b c s", b=B, s=2)
        junk = sb("junk", [128, 512], BF16)
        maps = sb("maps", [128, 6, 512], BF16)
        p_al = [ps(f"p_al{k}", [128, 512]) for k in range(2)]
        p_z = ps("p_z", [128, 512])
        p_y = [ps(f"p_y{k}", [128, 512]) for k in range(2)]
        p_v = ps("p_v", [128, 512])
        block = mem.enter_context(nc.Block())

        @block.sync
        def _(sp):
            sp = Sync(sp, c_in)
            row = lambda a, n: a.unsqueeze(0).to_broadcast((128, n))
            macc = io["macc"].rearrange("h i -> (h i)")
            st_v = stats.rearrange("b s h i -> b s (h i)")
            sp.dma_start(mrow[:], row(macc, C)).then_inc(c_in, 16)
            sp.dma_start(misc[:], cst["misc"]).then_inc(c_in, 16)
            with nc.allow_non_contiguous_dma(reason="a few thousand scalars, one to a partition"):
                for s in range(2):
                    sp.dma_start(mcol[s::2, :], macc.unsqueeze(1)).then_inc(c_in, 16)
                    sp.dma_start(rcol[s::2, :], st_v[:, 0].rearrange("b c -> c b")).then_inc(c_in, 16)
            sp.dma_start(srow[:].rearrange("p b s c -> p (b s c)"), row(stats.rearrange("b s h i -> (b s h i)"), B * 3 * C)).then_inc(c_in, 16)
            sp.dma_start(brow[:], row(bias, C)).then_inc(c_in, 16)
            sp.dma_start(grow[:, 1:C], row(io["gamma"], C - 1)).then_inc(c_in, 16)
            sp.dma_start(btrow[:, 1:C], row(io["beta"], C - 1)).then_inc(c_in, 16)
            sp.dma_start(idft_h[:], cst["idft_h"]).then_inc(c_in, 16)
            sp.dma_start(idft_w[:], cst["idft_w"]).then_inc(c_in, 16)
            sp.dma_start(ones[:], cst["sel"][:, 0]).then_inc(c_in, 16)

            def load(b, t):
                if not (is_at(b, 0) and t < NX):
                    sp.wait_ge(al_mm, b * 2 * T + 2 * (t - NX) + 2)
                sp.dma_start(xt[t % NX][:], x_v[b, t]).then_inc(x_in[t % NX], 16)

            for t in range(T):
                load(0, t)
            with sp.Fori(1, B) as b:
                for t in range(T):
                    load(b, t)

        @block.tensor
        def _(pe):
            def contract(b, t):
                pe.wait_ge(x_in[t % NX], b * (16 * T // NX) + (t // NX) * 16 + 16)
                for k in range(2):
                    if not (is_at(b, 0) and t == 0):
                        pe.wait_ge(al_sb, b * 2 * T + 2 * t + k - 1)
                    for j in range(4):
                        at = 2048 * k + 512 * j
                        last = nc.tensor.matmul(p_al[k][32 * j:32 * j + 32, :], awc[:], xt[t % NX][:, at:at + 512], start=True, stop=True)
                    last.then_inc(al_mm, 1)

            def layer(b):
                pe.wait_ge(v_ready, b * 2 + 2)
                if not is_at(b, 0):
                    pe.wait_ge(z_sb, b)
                for q in range(2):
                    last = nc.tensor.matmul(p_z[0:M2, 256 * q:256 * q + 256], vm[:, q], idft_h[:], start=True, stop=True)
                last.then_inc(z_mm, 1)
                pe.wait_ge(z_sb, b + 1)
                if not is_at(b, 0):
                    pe.wait_ge(alpha, b * 2)
                for q in range(2):
                    for s in range(2):
                        last = nc.tensor.matmul(p_y[q][:, 256 * s:256 * s + 256], zs[:, q, 128 * s:128 * s + 128], idft_w[0:M2], start=True, stop=True)
                last.then_inc(y_mm, 1)

            def entry(b):
                pe.wait_ge(w_ready, b + 1)
                for t in range(T):
                    contract(b, t)
                    if t == T - 2:
                        layer(b)

            pe.wait_ge(c_in, 16 * 13)
            entry(0)
            with pe.Fori(1, B) as b:
                entry(b)
            pe.wait_ge(var_in, 1)
            nc.tensor.matmul(p_v[:, 0:1], ones[:], sc[:, 8:9], start=True, stop=True).then_inc(var_mm, 1)

        @block.scalar
        def _(act):
            S = nc.scalar

            def copy_alpha(b, t):
                for k in range(2):
                    act.wait_ge(al_mm, b * 2 * T + 2 * t + k + 1)
                    if t % (T // 2) == 0 and k == 0 and not is_at(b, 0):
                        act.wait_ge(al_out[2 * t // T], b * 32)
                    S.activation(al_r[:, 2 * t + k], p_al[k][:], ACT.Copy).then_inc(al_sb, 1)

            def store_alpha(b, half):
                act.wait_ge(al_sb, b * 2 * T + (half + 1) * T)
                for s in range(2):
                    act.dma_start(al_rows[b, s][:, half * T:half * T + T], al_r[s::32, half * T:half * T + T]).then_inc(al_out[half], 16)

            def copy_z(b):
                act.wait_ge(z_mm, b + 1)
                if not is_at(b, 0):
                    act.wait_ge(y_mm, b)
                S.activation(zs[:].rearrange("m q h -> m (q h)"), p_z[0:M2, :], ACT.Copy).then_inc(z_sb, 1)

            def distances(b):
                act.wait_ge(squares_ready, b * 2 + 1)
                S.activation(w1[:], t1[:], ACT.Sqrt, bias=minus1[:]).then_inc(roots, 1)
                act.wait_ge(squares_ready, b * 2 + 2)
                S.activation(w2[:], t2[:], ACT.Sqrt).then_inc(roots, 1)
                act.wait_ge(e_ready, b + 1)
                S.activation(dist[:], t1[:], ACT.Ln).then_inc(logs, 1)
                act.wait_ge(logs, b + 1)
                if not is_at(b, 0):
                    act.wait_ge(dsum_ready, b)
                S.activation(junk[:], dist[:], ACT.Square, accum_out=dsum[:, b:b + 1] if isinstance(b, int) else dsum[:, bass.ds(b, 1)]).then_inc(dsum_ready, 1)

            def entry(b):
                for t in range(T):
                    copy_alpha(b, t)
                    if t == T // 2 - 1:
                        store_alpha(b, 0)
                        if not is_at(b, 0):
                            distances(b - 1)
                    if t == T - 2:
                        copy_z(b)
                store_alpha(b, 1)

            act.wait_ge(setup, 3)
            entry(0)
            with act.Fori(1, B) as b:
                entry(b)
            distances(B - 1)

        @block.gpsimd
        def _(pool):
            P = nc.gpsimd

            def weights(b):
                if not is_at(b, 0):
                    pool.wait_ge(al_mm, b * 2 * T)
                P.tensor_copy(awc[:], aw[:, b]).then_inc(w_ready, 1)

            def load_modes(b):
                if not is_at(b, 0):
                    pool.wait_ge(sp_used, b)
                for k in range(2):
                    pool.dma_start(spt[KX * k:KX * k + KX].rearrange("k (h i) m -> k h (i m)", h=HEADS),
                                   spec[b, k].rearrange("(h k) n -> k h n", h=HEADS)).then_inc(sp_in, 16)

            def load_dense(b):
                if not is_at(b, 0):
                    pool.wait_ge(alpha, b * 2)
                pool.dma_start(x0d[:].rearrange("p (s w) -> p s w", s=2), x0_v[b, 0]).then_inc(x0_in, 16)
                for half in range(2):
                    pool.wait_ge(al_out[half], b * 32 + 32)
                pool.dma_start(ald[:].rearrange("p (s w) -> p s w", s=2), al_v[b]).then_inc(al_in, 16)

            def store_dense(b):
                pool.wait_ge(maps_ready, b + 1)
                pool.dma_start(io["maps"][b].rearrange("m s (h w) -> h (m s) w", w=W), maps[:].rearrange("p m (s w) -> p (m s) w", s=2)).then_inc(maps_out, 16)
                pool.dma_start(io["bmap"][b].rearrange("s (h w) -> h s w", w=W), beta[:].rearrange("p (s w) -> p s w", s=2)).then_inc(beta_out, 16)
                pool.dma_start(io["x10"][b].rearrange("s (h w) -> h s w", w=W), x10[:].rearrange("p (s w) -> p s w", s=2)).then_inc(x10_out, 16)

            def entry(b):
                weights(b)
                load_modes(b)
                load_dense(b - 1)
                store_dense(b - 1)

            P.memset(sc[:, 12:13], -0.5).then_inc(setup, 1)
            P.memset(sc[:, 13:14], 0.5).then_inc(setup, 1)
            P.memset(minus1[:], -1.0).then_inc(setup, 1)
            pool.wait_ge(setup, 3)
            pool.wait_ge(mean_ready, 1)
            P.tensor_tensor(sc[:, 3:4], sc[:, 2:3], sc[:, 12:13], ALU.pow).then_inc(pow_done, 1)
            pool.wait_ge(aw_ready, 1)
            weights(0)
            load_modes(0)
            pool.wait_ge(uw_ready, 1)
            pool.dma_start(io["uws"].rearrange("b r c -> r b c"), uw[96:99].rearrange("p b c s -> p b (c s)")).then_inc(uw_out, 16)
            entry(1)
            with pool.Fori(2, B) as b:
                entry(b)
            load_dense(B - 1)
            store_dense(B - 1)
            pool.wait_ge(var_ready, 1)
            P.tensor_tensor(sc[:, 10:11], sc[:, 9:10], sc[:, 13:14], ALU.pow).then_inc(std_ready, 1)
            pool.wait_ge(uw_out, 16)
            pool.wait_ge(maps_out, B * 16)
            pool.wait_ge(beta_out, B * 16)
            pool.wait_ge(x10_out, B * 16)

        @block.vector
        def _(dve):
            V = nc.vector
            ch = Chain(dve, chain)
            s1 = lambda k: sc[:, k:k + 1]
            over_b = lambda a: a.unsqueeze(1).to_broadcast((128, B, C))

            def combine(b):
                dve.wait_ge(sp_in, b * 32 + 32)
                a = arow[0:64, b].rearrange("p c -> p c") if isinstance(b, int) else arow[0:64, b]
                ch.step(V.tensor_tensor(prod[:], spt[:], a.unsqueeze(2).to_broadcast((64, C, M2)), ALU.mult))
                if not is_at(b, 0):
                    dve.wait_ge(z_mm, b)
                V.tensor_reduce(vm[0:64, 0], prod[:].rearrange("p c m -> p m c"), AX_X, ALU.add).then_inc(v_ready, 1)
                V.tensor_copy(vm[0:64, 1], spt[:, 0]).then_inc(v_ready, 1)
                dve.wait_ge(v_ready, b * 2 + 2)
                V.memset(sc[:, 14:15], 0.0).then_inc(sp_used, 1)
                dve.wait_ge(sp_used, b + 1)

            def col(a, b):
                return a[:, b:b + 1] if isinstance(b, int) else a[:, bass.ds(b, 1)]

            def dense(b):
                dve.wait_ge(x0_in, b * 16 + 16)
                dve.wait_ge(al_in, b * 16 + 16)
                dve.wait_ge(y_mm, b + 1)
                if not is_at(b, 0):
                    dve.wait_ge(x10_out, b * 16)
                    dve.wait_ge(beta_out, b * 16)
                    dve.wait_ge(maps_out, b * 16)
                V.scalar_tensor_tensor(out=x10[:], in0=x0d[:], scalar=brow[:, 0:1], in1=p_y[1][:], op0=ALU.add, op1=ALU.add).then_inc(alpha, 1)
                V.tensor_tensor(t1[:], ald[:], p_y[0][:], ALU.add).then_inc(alpha, 1)
                dve.wait_ge(alpha, b * 2 + 2)
                ch.step(V.tensor_scalar(al[:], t1[:], col(ac, b), 1.0 + EPS, ALU.add, ALU.max))
                V.tensor_tensor(t1[:], al[:], al[:], ALU.mult).then_inc(squares_ready, 1)
                ch.step(V.tensor_scalar(t2[:], al[:], 1.0, None, ALU.subtract))
                V.scalar_tensor_tensor(out=t2[:], in0=al[:], scalar=1.0, in1=t2[:], op0=ALU.add, op1=ALU.mult).then_inc(squares_ready, 1)
                ch.step(V.tensor_scalar(coef[:], x10[:], col(q2, b), col(q3, b), ALU.mult, ALU.add))
                ch.step(V.scalar_tensor_tensor(out=beta[:], in0=al[:], scalar=s1(5), in1=coef[:], op0=ALU.mult, op1=ALU.add))
                dve.wait_ge(roots, b * 2 + 2)
                V.tensor_tensor(t1[:], al[:], w2[:], ALU.add).then_inc(e_ready, 1)
                ch.step(V.reciprocal(t2[:], w1[:]))
                dve.wait_ge(logs, b + 1)
                ch.step(V.tensor_tensor(coef[:], dist[:], t2[:], ALU.mult))
                both = ((coef, 0, w1), (beta, 1, w2))
                for v, k, r in both:
                    ch.inc(V.tensor_copy(maps[:, k], v[:]))
                ch.wait()
                for v, k, r in both:
                    ch.inc(V.tensor_tensor(r[:], v[:], maps[:, k], ALU.subtract))
                ch.wait()
                for v, k, r in both:
                    ch.inc(V.tensor_copy(maps[:, 2 + k], r[:]))
                ch.wait()
                ch.inc(V.tensor_tensor(maps[:, 4], w1[:], maps[:, 2], ALU.subtract))
                V.tensor_tensor(maps[:, 5], w2[:], maps[:, 3], ALU.subtract).then_inc(maps_ready, 1)
                ch.wait()
                dve.wait_ge(maps_ready, b + 1)

            def split(v, r):
                ch.step(V.tensor_copy(vp[0][:], v[:]))
                ch.step(V.tensor_tensor(r[:], v[:], vp[0][:], ALU.subtract))
                ch.step(V.tensor_copy(vp[1][:], r[:]))
                ch.step(V.tensor_tensor(vp[2][:], r[:], vp[1][:], ALU.subtract))

            def place(out, v, at, add, tmp):
                vv = v[:].rearrange("p b c -> p (b c)").unsqueeze(2).to_broadcast((128, B * C, 2))
                mask = misc[:, at:at + 2].unsqueeze(1).to_broadcast((128, B * C, 2))
                flat = lambda t: t.rearrange("p b c s -> p (b c) s")
                if not add:
                    return ch.step(V.tensor_tensor(flat(out), vv, mask, ALU.mult))
                ch.step(V.tensor_tensor(flat(tmp), vv, mask, ALU.mult))
                ch.step(V.tensor_tensor(out.rearrange("p b c s -> p b (c s)"), out.rearrange("p b c s -> p b (c s)"), tmp.rearrange("p b c s -> p b (c s)"), ALU.add))

            ch.inc(V.memset(grow[:, 0:1], 0.0))
            ch.inc(V.memset(btrow[:, 0:1], 0.0))
            ch.inc(V.memset(aw[:], 0.0))
            ch.inc(V.memset(vm[:], 0.0))
            dve.wait_ge(c_in, 16 * 13)
            ch.inc(V.tensor_scalar(mrow[:], mrow[:], 1.0 / B, None, ALU.mult))
            ch.step(V.tensor_scalar(mcol[:], mcol[:], 1.0 / B, None, ALU.mult))
            ch.step(V.tensor_tensor(msr[:], mrow[:], mrow[:], ALU.mult))
            ch.step(V.tensor_reduce(s1(0), msr[:, 1:C], AX_X, ALU.add))
            ch.step(V.tensor_tensor(s1(1), msr[:, 0:1], s1(0), ALU.subtract))
            V.tensor_scalar(s1(2), s1(1), EPS, None, ALU.max).then_inc(mean_ready, 1)
            dve.wait_ge(pow_done, 1)
            ch.inc(V.tensor_scalar(mrow[:], mrow[:], s1(3), None, ALU.mult))
            ch.step(V.scalar_tensor_tensor(out=mcol[:], in0=mcol[:], scalar=s1(3), in1=misc[:, 10:11], op0=ALU.mult, op1=ALU.mult))
            for s in range(2):
                V.scalar_tensor_tensor(out=aw[:, :, s], in0=rcol[:], scalar=mcol[:], in1=misc[:, 8 + s:9 + s].to_broadcast((128, B)), op0=ALU.mult, op1=ALU.mult).then_inc(*((aw_ready, 1) if s else (setup, 1)))
            ch.inc(V.tensor_scalar(s1(4), mrow[:, 0:1], 1.0, None, ALU.add))
            ch.step(V.tensor_scalar(msr[:], mrow[:], -1.0, None, ALU.mult))
            ch.inc(V.reciprocal(s1(5), s1(4)))
            ch.step(V.tensor_copy(msr[:, 0:1], mrow[:, 0:1]))
            ch.inc(V.tensor_tensor(arow[:], srow[:, :, 0], over_b(msr[:]), ALU.mult))
            ch.step(V.tensor_tensor(v1[:], over_b(brow[:]), srow[:, :, 1], ALU.subtract))
            ch.inc(V.tensor_tensor(v2[:], v1[:], arow[:], ALU.mult))
            ch.step(V.tensor_scalar(q2[:], srow[:, :, 0, 0], s1(5), None, ALU.mult))
            ch.inc(V.tensor_reduce(ac[:], v2[:], AX_X, ALU.add))
            ch.step(V.scalar_tensor_tensor(out=q3[:], in0=srow[:, :, 1, 0], scalar=-1.0, in1=q2[:], op0=ALU.mult, op1=ALU.mult))
            combine(0)
            place(uw[:], v1, 32, False, None)
            ch.step(V.tensor_tensor(v2[:], srow[:, :, 2], over_b(mrow[:]), ALU.mult))
            place(wide, v2, 30, False, None)
            V.tensor_tensor(uw[:].rearrange("p b c s -> p b (c s)"), uw[:].rearrange("p b c s -> p b (c s)"), wide.rearrange("p b c s -> p b (c s)"), ALU.add).then_inc(uw_ready, 1)
            lw = keep["lw"]
            split(v2, v1)
            for part in range(3):
                place(lw[1][:], vp[part], 18 + 2 * part, part > 0, wt[:])
            ch.step(V.tensor_tensor(v2[:], srow[:, :, 1], over_b(btrow[:]), ALU.add))
            split(v2, v1)
            for part in range(3):
                place(lw[1][:], vp[part], 24 + 2 * part, True, wt[:])
            ch.step(V.tensor_tensor(v2[:], srow[:, :, 0], over_b(grow[:]), ALU.mult))
            split(v2, v1)
            for part in range(3):
                place(lw[0][:], vp[part], 12 + 2 * part, part > 0, wt[:])
            with dve.Fori(1, B) as b:
                ch.loop(b, 1, PER_B)
                combine(b)
                dense(b - 1)
                ch.end(B - 1)
            dense(B - 1)
            dve.wait_ge(dsum_ready, B)
            V.tensor_reduce(s1(8), dsum[:], AX_X, ALU.add).then_inc(var_in, 1)
            dve.wait_ge(var_mm, 1)
            V.tensor_scalar(s1(9), p_v[:, 0:1], 1.0 / (B * N), None, ALU.mult).then_inc(var_ready, 1)
            dve.wait_ge(std_ready, 1)
            ch.step(V.tensor_scalar(s1(11), s1(10), EPS, None, ALU.add))
            ch.step(V.reciprocal(keep["k"][:], s1(11)))


PER_B = 14


def stage_c(nc, ctx, io, B, keep):
    x, spec, cst, out = io["x"], io["spec"], io["cst"], io["out"]
    sem = lambda n: ctx.enter_context(nc.semaphore("c_" + n))
    T = HALF // TC
    ROWS = TC // W
    CH = 4
    TCH = T // CH
    GR = 2 * T
    flat = lambda a: a.rearrange("b c h w -> b (c h w)").rearrange("b (p t n) -> b t p n", p=128, t=T)
    x_v, o_v = flat(x), flat(out)
    o0_v = out.rearrange("b c (s h) w -> b c h s w", s=2)
    maps_v = io["maps"].rearrange("b m s (t n) -> b t (m s) n", n=TC)
    bmap_v = io["bmap"].rearrange("b s (t n) -> b t s n", n=TC)
    ts_rows = io["tsum"].rearrange("b s (k j n) -> b s j k n", j=4, n=512)
    dense = lambda a: a.rearrange("b s (h w) -> b h s w", w=W)
    x_in = [sem(f"x_in{k}") for k in range(4)]
    o_out = [sem(f"o_out{k}") for k in range(4)]
    r_in = [sem(f"r_in{k}") for k in range(2)]
    ys_in = [sem(f"ys_in{k}") for k in range(2)]
    u_in = [sem(f"u_in{k}") for k in range(2)]
    tr_out = [sem(f"tr_out{k}") for k in range(2)]
    c_in, first_zero, zeroed, filled = sem("c_in"), sem("first_zero"), sem("zeroed"), sem("filled")
    z_mm, z_sb = sem("z_mm"), sem("z_sb")
    u_mm, g_mm, p_mm, t_mm = sem("u_mm"), sem("g_mm"), sem("p_mm"), sem("t_mm")
    u_done, s_done, v_done, o_done, sq_done, tr_sb = sem("u_done"), sem("s_done"), sem("v_done"), sem("o_done"), sem("sq_done"), sem("tr_sb")
    td_in, x10_in, th_ready, o0_ready, o0_out = sem("td_in"), sem("x10_in"), sem("th_ready"), sem("o0_ready"), sem("o0_out")

    with ExitStack() as mem:
        sb = lambda n, s, d=FP32: mem.enter_context(nc.sbuf_tensor("c_" + n, s, d))
        ps = lambda n, s: mem.enter_context(nc.psum_tensor("c_" + n, s, FP32))
        xt = [sb(f"xt{k}", [128, TC]) for k in range(4)]
        ot = [sb(f"ot{k}", [128, TC]) for k in range(4)]
        rt = [sb(f"rt{k}", [128, TC], BF16) for k in range(2)]
        mv = [sb(f"mv{k}", [128, TC]) for k in range(2)]
        zc = [sb(f"zc{k}", [128, 32, 2 * C]) for k in range(2)]
        ys = sb("ys", [128, C, M2])
        u = [sb(f"u{k}", [128, 1024]) for k in range(2)]
        s0 = [sb(f"s0{k}", [128, 1024]) for k in range(2)]
        sq = [sb(f"sq{k}", [128, 1024]) for k in range(2)]
        tr = sb("tr", [128, T, 512])
        td, th, x10, o0 = (sb(n, [128, 512]) for n in ("td", "th", "x10", "o0"))
        idft_h = sb("idft_h", [128, H])
        misc = sb("misc", [128, 48])
        halves = sb("halves", [128, 32])
        btcol = sb("btcol", [128, 1])
        p_u, p_g, p_p = ps("p_u", [128, 1024]), ps("p_g", [128, 1024]), ps("p_p", [128, 1024])
        p_z, p_t = ps("p_z", [128, 512]), ps("p_t", [128, 512])
        block = mem.enter_context(nc.Block())

        @block.sync
        def _(sp):
            sp = Sync(sp, c_in)

            def load_x(b, t):
                if t >= T:
                    b, t = b + 1, t - T
                if not (is_at(b, 0) and t < 4):
                    sp.wait_ge(u_done, b * GR + 2 * t - 6)
                sp.dma_start(xt[t % 4][:], x_v[b, t]).then_inc(x_in[t % 4], 16)

            def load_maps(b, t):
                if not (is_at(b, 0) and t < 2):
                    sp.wait_ge(p_mm, b * GR + 2 * t - 2)
                sp.dma_start(rt[t % 2][0:12], maps_v[b, t]).then_inc(r_in[t % 2], 16)
                sp.dma_start(rt[t % 2][12:20], maps_v[b, t, 0:8]).then_inc(r_in[t % 2], 16)
                sp.dma_start(rt[t % 2][20:24], maps_v[b, t, 0:4]).then_inc(r_in[t % 2], 16)
                sp.dma_start(mv[t % 2][96:98], bmap_v[b, t]).then_inc(r_in[t % 2], 16)

            def store(b, t):
                if t < 0:
                    b, t = b - 1, t + T
                sp.wait_ge(o_done, b * GR + 2 * t + 2)
                sp.dma_start(o_v[b, t], ot[t % 4][:]).then_inc(o_out[t % 4], 16)

            def load_modes(b, half):
                for k in range(2):
                    sp.dma_start(ys[KX * k:KX * k + KX, 32 * half:32 * half + 32].rearrange("k (h i) m -> k h (i m)", h=2),
                                 spec[b, k].rearrange("(h k) n -> k h n", h=HEADS)[:, 2 * half:2 * half + 2]).then_inc(ys_in[half], 16)

            def load_urows(b, k):
                sp.dma_start(zc[k][96:99], io["uws"][b].unsqueeze(1).to_broadcast((3, 32, 2 * C))).then_inc(u_in[k], 16)

            def store_sums(b, half):
                sp.wait_ge(tr_sb, b * T + 8 * half + 8)
                for s in range(2):
                    sp.dma_start(ts_rows[b, s][:, 8 * half:8 * half + 8], tr[s::32, 8 * half:8 * half + 8]).then_inc(tr_out[half], 16)

            def load_sums(b):
                for half in range(2):
                    sp.wait_ge(tr_out[half], b * 32 + 32)
                if not is_at(b, 0):
                    sp.wait_ge(th_ready, b)
                sp.dma_start(td[:].rearrange("p (s w) -> p s w", s=2), dense(io["tsum"])[b]).then_inc(td_in, 16)

            def load_x10(b):
                if not is_at(b, 0):
                    sp.wait_ge(o0_ready, b)
                sp.dma_start(x10[:].rearrange("p (s w) -> p s w", s=2), dense(io["x10"])[b]).then_inc(x10_in, 16)

            def store_channel_0(b):
                sp.wait_ge(o0_ready, b + 1)
                for k in range(4):
                    sp.wait_ge(o_out[k], b * 64 + 64)
                sp.dma_start(o0_v[b, 0], o0[:].rearrange("p (s w) -> p s w", s=2)).then_inc(o0_out, 16)

            def entry(b, last=False):
                for t in range(T):
                    load_maps(b, t)
                    if not (last and t + 2 >= T):
                        load_x(b, t + 2)
                    if not (is_at(b, 0) and t < 3):
                        store(b, t - 3)
                    if not is_at(b, 0):
                        if t == 1:
                            sp.wait_ge(u_mm, b * GR)
                            load_urows(b, 1)
                            store_sums(b - 1, 1)
                            load_x10(b - 1)
                        if t == 3:
                            load_sums(b - 1)
                        if t == 7:
                            store_channel_0(b - 1)
                    if t == 9:
                        store_sums(b, 0)
                    if not last:
                        if t in (11, 12):
                            half = t - 11
                            sp.wait_ge(z_mm, b * GR + 28 + 4 * half)
                            load_modes(b + 1, half)
                        if t == 13:
                            sp.wait_ge(u_mm, b * GR + 24)
                            load_urows(b + 1, 0)

            sp.wait_ge(zeroed, 9)
            for k in range(2):
                sp.dma_start(mv[k][0:M2].rearrange("p (r w) -> p r w", w=W), cst["idft_w"][0:M2].unsqueeze(1).to_broadcast((M2, ROWS, W))).then_inc(c_in, 16)
            sp.dma_start(idft_h[:], cst["idft_h"]).then_inc(c_in, 16)
            sp.dma_start(misc[:], cst["misc"]).then_inc(c_in, 16)
            with nc.allow_non_contiguous_dma(reason="63 scalars, one to a partition"):
                for s in range(2):
                    sp.dma_start(btcol[2 + s::2, :], io["beta"].unsqueeze(1)).then_inc(c_in, 16)
            for half in range(2):
                load_modes(0, half)
            for k in range(2):
                load_urows(0, k)
            load_x(0, 0)
            load_x(0, 1)
            entry(0)
            with sp.Fori(1, B - 1) as b:
                entry(b)
            entry(B - 1, last=True)
            for t in range(3):
                store(B, t - 3)
            store_sums(B - 1, 1)
            load_x10(B - 1)
            load_sums(B - 1)
            store_channel_0(B - 1)
            sp.wait_ge(o0_out, B * 16)

        @block.tensor
        def _(pe):
            def modes_part(chunk, part, wait):
                pe.wait_ge(z_sb, wait)
                for c in range(8):
                    last = nc.tensor.matmul(p_z[0:M2, 64 * c:64 * c + 64], ys[:, 8 * part + c], idft_h[:].rearrange("p (s h) -> p s h", s=2)[:, :, 32 * chunk:32 * chunk + 32], start=True, stop=True)
                last.then_inc(z_mm, 1)

            def sums(b, t, n):
                if n < 0:
                    b, t, n = (b, t - 1, 1) if t else (b - 1, T - 1, 1)
                g = b * GR + 2 * t + n
                pe.wait_ge(sq_done, g + 1)
                if n == 0 and not (is_at(b, 0) and t == 0):
                    pe.wait_ge(tr_sb, b * T + t)
                for j in range(2):
                    at = 32 * (2 * n + j)
                    last = nc.tensor.matmul(p_t[at:at + 32, :], halves[:], sq[n][:, 512 * j:512 * j + 512], start=True, stop=True)
                last.then_inc(t_mm, 1)

            def group(b, t, n, last):
                g = b * GR + 2 * t + n
                ck, gi = t // TCH, 2 * (t % TCH) + n
                first = is_at(b, 0) and t == 0 and n == 0
                if n == 0:
                    pe.wait_ge(r_in[t % 2], b * (64 * T // 2) + 64 * (t // 2) + 64)
                if gi == 0:
                    pe.wait_ge(z_sb, b * GR + 8 * ck + 8)
                    if ck < 2:
                        pe.wait_ge(u_in[ck], b * 16 + 16)
                if not first:
                    pe.wait_ge(u_done, g)
                for r in range(4):
                    row = 4 * n + r
                    ins = nc.tensor.matmul(p_u[:, W * r:W * r + W], zc[ck % 2][:, (t % TCH) * ROWS + row], mv[t % 2][:, W * row:W * row + W], start=True, stop=True)
                ins.then_inc(u_mm, 1)
                if not first:
                    pe.wait_ge(s_done, g)
                for k in range(2):
                    at = 1024 * n + 512 * k
                    ins = nc.tensor.matmul(p_g[:, 512 * k:512 * k + 512], lw(0, b), rt[t % 2][:, at:at + 512], start=True, stop=True)
                ins.then_inc(g_mm, 1)
                if not (last and ck == CH - 1):
                    if ck == CH - 1 and gi in (0, 4):
                        pe.wait_ge(ys_in[gi // 4], b * 32 + 64)
                    modes_part((ck + 1) % CH, gi, g + 8)
                if not first:
                    plus(b, t, n - 1)
                    sums(b, t, n - 1)

            def plus(b, t, n):
                if n < 0:
                    b, t, n = (b, t - 1, 1) if t else (b - 1, T - 1, 1)
                if not (is_at(b, 0) and t == 0 and n == 0):
                    pe.wait_ge(o_done, b * GR + 2 * t + n)
                for k in range(2):
                    at = 1024 * n + 512 * k
                    ins = nc.tensor.matmul(p_p[:, 512 * k:512 * k + 512], lw(1, b), rt[t % 2][:, at:at + 512], start=True, stop=True)
                ins.then_inc(p_mm, 1)

            def lw(k, b):
                return keep["lw"][k][:, b].rearrange("p c s -> p (c s)")

            def entry(b, last=False):
                for t in range(T):
                    for n in range(2):
                        group(b, t, n, last)

            pe.wait_ge(zeroed, 9)
            pe.wait_ge(c_in, 16 * 6)
            pe.wait_ge(filled, 1)
            for half in range(2):
                pe.wait_ge(ys_in[half], 32)
            for part in range(8):
                if part:
                    modes_part(0, part, part)
                else:
                    for c in range(8):
                        ins = nc.tensor.matmul(p_z[0:M2, 64 * c:64 * c + 64], ys[:, c], idft_h[:].rearrange("p (s h) -> p s h", s=2)[:, :, 0:32], start=True, stop=True)
                    ins.then_inc(z_mm, 1)
            entry(0)
            with pe.Fori(1, B - 1) as b:
                entry(b)
            entry(B - 1, last=True)
            plus(B - 1, T - 1, 1)
            sums(B - 1, T - 1, 1)

        @block.scalar
        def _(act):
            S = nc.scalar

            def copy_part(chunk_buffer, part, count):
                act.wait_ge(z_mm, count)
                S.activation(zc[chunk_buffer][0:M2, :, 16 * part:16 * part + 16].rearrange("m h c -> m c h"),
                             p_z[0:M2, :].rearrange("m (c h) -> m c h", h=32), ACT.Copy).then_inc(z_sb, 1)

            def copy_sums(b, t):
                if t < 0:
                    b, t = b - 1, T - 1
                act.wait_ge(t_mm, b * GR + 2 * t + 2)
                if t in (0, 8) and not is_at(b, 0):
                    act.wait_ge(tr_out[t // 8], b * 32)
                S.activation(tr[:, t], p_t[:], ACT.Copy).then_inc(tr_sb, 1)

            def root(b):
                act.wait_ge(td_in, b * 16 + 16)
                if not is_at(b, 0):
                    act.wait_ge(o0_ready, b)
                S.activation(th[:], td[:], ACT.Sqrt, bias=1.0).then_inc(th_ready, 1)

            def group(b, t, n, last):
                g = b * GR + 2 * t + n
                ck, gi = t // TCH, 2 * (t % TCH) + n
                if n == 1 and not (is_at(b, 0) and t == 0):
                    copy_sums(b, t - 1)
                if not (last and ck == CH - 1):
                    if gi == 0 and not (is_at(b, 0) and ck == 0):
                        act.wait_ge(u_mm, b * GR + 8 * ck)
                    copy_part((ck + 1) % 2, gi, g + 9)
                act.wait_ge(s_done, g + 1)
                if not (is_at(b, 0) and t == 0):
                    act.wait_ge(t_mm, g - 1)
                S.activation(sq[n][:], s0[n][:], ACT.Square, bias=btcol[:]).then_inc(sq_done, 1)

            def entry(b, last=False):
                for t in range(T):
                    for n in range(2):
                        group(b, t, n, last)
                    if t == 5 and not is_at(b, 0):
                        root(b - 1)

            act.wait_ge(zeroed, 9)
            act.wait_ge(c_in, 16 * 6)
            for part in range(8):
                copy_part(0, part, part + 1)
            entry(0)
            with act.Fori(1, B - 1) as b:
                entry(b)
            entry(B - 1, last=True)
            copy_sums(B - 1, T - 1)
            root(B - 1)

        @block.vector
        def _(dve):
            V = nc.vector

            def add_x(b, t, n):
                g = b * GR + 2 * t + n
                if n == 0:
                    dve.wait_ge(x_in[t % 4], b * (4 * T) + 16 * (t // 4) + 16)
                dve.wait_ge(u_mm, g + 1)
                if not (is_at(b, 0) and t == 0):
                    dve.wait_ge(v_done, g - 1)
                V.tensor_tensor(u[n][:], xt[t % 4][:, 1024 * n:1024 * n + 1024], p_u[:], ALU.add).then_inc(u_done, 1)

            def scale(b, t, n):
                g = b * GR + 2 * t + n
                dve.wait_ge(u_done, g + 1)
                dve.wait_ge(g_mm, g + 1)
                if not (is_at(b, 0) and t == 0):
                    dve.wait_ge(sq_done, g - 1)
                V.scalar_tensor_tensor(out=s0[n][:], in0=u[n][:], scalar=keep["k"][:], in1=p_g[:], op0=ALU.mult, op1=ALU.mult).then_inc(s_done, 1)

            def finish(b, t, n):
                if n < 0:
                    b, t, n = (b, t - 1, 1) if t else (b - 1, T - 1, 1)
                g = b * GR + 2 * t + n
                dve.wait_ge(v_done, g + 1)
                dve.wait_ge(p_mm, g + 1)
                o = ot[t % 4][:, 1024 * n:1024 * n + 1024]
                V.tensor_tensor(o, o, p_p[:], ALU.add).then_inc(o_done, 1)

            def entry(b):
                for t in range(T):
                    for n in range(2):
                        add_x(b, t, n)
                        scale(b, t, n)
                        if not (is_at(b, 0) and t == 0 and n == 0):
                            finish(b, t, n - 1)

            for t in zc:
                V.memset(t[:], 0.0).then_inc(zeroed, 1)
            V.memset(ys[:], 0.0).then_inc(zeroed, 1)
            V.memset(btcol[:], 0.0).then_inc(zeroed, 1)
            V.memset(halves[:], 0.0).then_inc(zeroed, 1)
            for t in rt:
                V.memset(t[:], 0.0).then_inc(first_zero, 1)
            dve.wait_ge(first_zero, 4)
            for t in rt:
                V.memset(t[32:35], 1.0).then_inc(zeroed, 1)
            dve.wait_ge(zeroed, 9)
            dve.wait_ge(c_in, 16 * 6)
            V.tensor_copy(halves[:, 0:2], misc[:, 8:10]).then_inc(filled, 1)
            entry(0)
            with dve.Fori(1, B) as b:
                entry(b)
            finish(B - 1, T - 1, 1)

        @block.gpsimd
        def _(pool):
            P = nc.gpsimd

            def add(b, t, n):
                g = b * GR + 2 * t + n
                pool.wait_ge(s_done, g + 1)
                if n == 0 and not (is_at(b, 0) and t < 4):
                    pool.wait_ge(o_out[t % 4], b * (4 * T) + 16 * (t // 4))
                P.tensor_tensor(ot[t % 4][:, 1024 * n:1024 * n + 1024], s0[n][:], u[n][:], ALU.add).then_inc(v_done, 1)

            def channel_0(b):
                pool.wait_ge(th_ready, b + 1)
                pool.wait_ge(x10_in, b * 16 + 16)
                if not is_at(b, 0):
                    pool.wait_ge(o0_out, b * 16)
                P.tensor_tensor(o0[:], th[:], x10[:], ALU.add).then_inc(o0_ready, 1)

            def entry(b):
                for t in range(T):
                    for n in range(2):
                        add(b, t, n)
                    if t == 6 and not is_at(b, 0):
                        channel_0(b - 1)

            for t in mv:
                P.memset(t[:], 0.0).then_inc(first_zero, 1)
            pool.wait_ge(first_zero, 4)
            for t in mv:
                P.memset(t[96:99], 1.0).then_inc(zeroed, 1)
            entry(0)
            with pool.Fori(1, B) as b:
                entry(b)
            channel_0(B - 1)



def program(nc, args, B):
    io = dict(args)
    dram = lambda n, s, d=FP32: nc.dram_tensor(n, s, d, kind="Internal").ap()
    with ExitStack() as ctx:
        io["spec"] = dram("spec", (B, 2, HEADS * KX, CI * M2))
        io["stats"] = dram("stats", (B, 3, HEADS, CI))
        io["macc"] = dram("macc", (HEADS, CI))
        io["alx"] = dram("alx", (B, 2, HALF))
        io["x10"] = dram("x10", (B, 2, HALF))
        io["bmap"] = dram("bmap", (B, 2, HALF))
        io["maps"] = dram("maps", (B, 6, 2, HALF), BF16)
        io["tsum"] = dram("tsum", (B, 2, HALF))
        io["uws"] = dram("uws", (B, 3, 2 * C))
        stage_a(nc, ctx, io, B)
        with ExitStack() as kept:
            sb = lambda n, s, d=FP32: kept.enter_context(nc.sbuf_tensor("keep_" + n, s, d))
            keep = {"lw": [sb(f"lw{k}", [128, B, C, 2], BF16) for k in range(2)], "k": sb("k", [128, 1])}
            stage_b(nc, ctx, io, B, keep)
            stage_c(nc, ctx, io, B, keep)


def arrays_of(x, w_re, w_im, bias, gamma, beta):
    import numpy as np
    re = np.asarray(w_re).transpose(0, 3, 2, 1, 4)
    im = np.asarray(w_im).transpose(0, 3, 2, 1, 4)
    wmix = np.stack([np.stack([re, im], 4), np.stack([im, re], 4)], 3)
    a = {"x": x, "wmix": wmix.reshape(HEADS * KX, -1), "bias": np.asarray(bias).reshape(C), "gamma": gamma, "beta": beta}
    a.update(constants())
    a["ident"] = np.eye(128, dtype=np.float32)
    return {k: np.ascontiguousarray(v) for k, v in a.items()}


def build(nc, arrays):
    aps = {}
    for name, a in arrays.items():
        aps[name] = nc.dram_tensor(f"in_{name}", a.shape, FP32, kind="ExternalInput").ap()
    B = arrays["x"].shape[0]
    io = {k: aps[k] for k in ("x", "wmix", "bias", "gamma", "beta")}
    io["cst"] = aps
    io["out"] = nc.dram_tensor("out", arrays["x"].shape, FP32, kind="ExternalOutput").ap()
    program(nc, io, B)


def kernel(x, L0_conv_weight_re, L0_conv_weight_im, L0_conv_bias, L1_conv_gamma, L1_conv_beta):
    import concourse.bacc as bacc
    from concourse.bass_utils import run_bass_kernel_spmd
    arrays = arrays_of(x, L0_conv_weight_re, L0_conv_weight_im, L0_conv_bias, L1_conv_gamma, L1_conv_beta)
    nc = bacc.Bacc("TRN2", target_bir_lowering=False, num_devices=1)
    build(nc, arrays)
    r = run_bass_kernel_spmd(nc, [{f"in_{k}": v for k, v in arrays.items()}], core_ids=[0])
    return r.results[0]["out"]
```
